# Optimizing a Trainium2 kernel written in Bass

```python
import numpy as np
import jax
import jax.numpy as jnp

def _softmax(x, axis=-1):
    return jax.nn.softmax(x, axis=axis)

def _gelu(x):
    return jax.nn.gelu(x, approximate=True)

def _silu(x):
    return jax.nn.silu(x)

def _sigmoid(x):
    return jax.nn.sigmoid(x)

def _layernorm(x, axis=-1, eps=1e-05):
    m = jnp.mean(x, axis=axis, keepdims=True)
    v = jnp.var(x, axis=axis, keepdims=True)
    return (x - m) / jnp.sqrt(v + eps)

def _scatter_add(tgt, idx, src, axis=0):
    return tgt.at[idx].add(src)

def _segment_sum(src, seg, n):
    return jax.ops.segment_sum(src, seg, n)
kernel_name = 'mk_adaln_ffn_d1_seqx_r4_47fe99'

def setup_inputs(seed: int=0):
    np.random.seed(seed)
    _w = jnp.asarray

    def _rec_inputs():
        import jax
        import jax.numpy as jnp
        _rk = jax.random.key(seed)
        x = -0.000125 + 0.9999 * jax.random.normal(jax.random.fold_in(_rk, 1), (2, 1024, 256), jnp.float32)
        _lenS = 1024 - jax.random.randint(jax.random.fold_in(_rk, 7), (2,), 0, max(1, 1024 // 4) + 1, jnp.int32)
        _lenS2 = 1024 - jax.random.randint(jax.random.fold_in(_rk, 8), (2,), 0, max(1, 1024 // 4) + 1, jnp.int32)
        cond_1024 = -0.00495105 + 0.998799 * jax.random.normal(jax.random.fold_in(_rk, 11), (2, 256), jnp.float32)
        return (x, cond_1024)
    x, cond_1024 = _rec_inputs()

    def _L0_cond_setup():
        import jax, jax.numpy as jnp
        import numpy as np
        B, L, D_IN, D = (64, 128, 256, 256)
        key = jax.random.key(seed)
        k1, k2, k3, k4, k5 = jax.random.split(key, 5)
        x = jax.random.normal(k1, (B, L, D_IN), dtype=jnp.float32)
        Wk = jax.random.normal(k2, (D_IN, 3 * D), dtype=jnp.float32) * (1.0 / np.sqrt(D_IN))
        Wr = jax.random.normal(k3, (D, 3 * D), dtype=jnp.float32) * (1.0 / np.sqrt(D))
        c0 = jax.random.normal(k4, (B, D), dtype=jnp.float32)
        h0 = jax.random.normal(k5, (B, D), dtype=jnp.float32)
        return {'x': x, 'Wk': Wk, 'Wr': Wr, 'c0': c0, 'h0': h0}
    _L0_cond_all = _L0_cond_setup()
    _L0_cond_in = {k: v for k, v in _L0_cond_all.items() if k in ('Wk', 'Wr')}
    del _L0_cond_all

    def _L0_ffn_setup():
        import jax, jax.numpy as jnp
        import numpy as np
        HIDDEN = 256
        INTER = 1024
        key = jax.random.key(seed)
        k1, k2, k3, k4, k5 = jax.random.split(key, 5)
        hidden_states = jax.random.normal(k1, (4, 512, HIDDEN), dtype=jnp.float32)
        W1 = jax.random.normal(k2, (HIDDEN, INTER), dtype=jnp.float32) * (1.0 / np.sqrt(HIDDEN))
        b1 = jax.random.normal(k3, (INTER,), dtype=jnp.float32) * 0.02
        W2 = jax.random.normal(k4, (INTER, HIDDEN), dtype=jnp.float32) * (1.0 / np.sqrt(INTER))
        b2 = jax.random.normal(k5, (HIDDEN,), dtype=jnp.float32) * 0.02
        return {'hidden_states': hidden_states, 'W1': W1, 'b1': b1, 'W2': W2, 'b2': b2}
    _L0_ffn_all = _L0_ffn_setup()
    _L0_ffn_in = {k: v for k, v in _L0_ffn_all.items() if k in ('W1', 'b1', 'W2', 'b2')}
    del _L0_ffn_all
    return {'x': x, 'cond_1024': cond_1024, 'L0_cond_Wk': _L0_cond_in['Wk'], 'L0_cond_Wr': _L0_cond_in['Wr'], 'L0_ffn_W1': _L0_ffn_in['W1'], 'L0_ffn_b1': _L0_ffn_in['b1'], 'L0_ffn_W2': _L0_ffn_in['W2'], 'L0_ffn_b2': _L0_ffn_in['b2']}

def reference(x, cond_1024, L0_cond_Wk, L0_cond_Wr, L0_ffn_W1, L0_ffn_b1, L0_ffn_W2, L0_ffn_b2):
    import jax
    import jax.numpy as jnp

    def _L0_cond_ref(x, Wk, Wr, c0, h0):
        import jax, jax.numpy as jnp
        import numpy as np
        B, L, D_IN, D = (64, 128, 256, 256)
        x_proj = jnp.einsum('bli,ig->blg', x, Wk)

        def step(carry, xp_t):
            c, h = carry
            gates = xp_t + h @ Wr
            f, o, g = jnp.split(gates, 3, axis=-1)
            sf = jax.nn.sigmoid(f)
            c_new = c * sf + (1.0 - sf) * jnp.tanh(g)
            h_new = jax.nn.sigmoid(o) * jnp.tanh(c_new)
            return ((c_new, h_new), h_new)
        _, hs = jax.lax.scan(step, (c0, h0), jnp.swapaxes(x_proj, 0, 1))
        return jnp.swapaxes(hs, 0, 1)

    def _L0_ffn_ref(hidden_states, W1, b1, W2, b2):
        import jax, jax.numpy as jnp
        import numpy as np
        HIDDEN = 256
        INTER = 1024
        h = jax.nn.relu(jnp.einsum('bsh,hi->bsi', hidden_states, W1) + b1)
        return jnp.einsum('bsi,ih->bsh', h, W2) + b2
    x = x + _L0_ffn_ref(_L0_cond_ref(x, L0_cond_Wk, L0_cond_Wr, cond_1024, cond_1024), L0_ffn_W1, L0_ffn_b1, L0_ffn_W2, L0_ffn_b2)
    return x

_drawn_inputs = setup_inputs


def setup_inputs(seed=0):
    import zlib

    import numpy as np

    out = dict(_drawn_inputs(seed))
    spreads = {}
    factors = {'cond_1024': 8.0, 'L0_ffn_b1': 4.134, 'L0_ffn_b2': 2.939}
    for name, (base, spread) in spreads.items():
        noise = np.random.default_rng([zlib.crc32(name.encode()), seed]).standard_normal(out[name].shape)
        drawn = base * np.exp(spread * noise) if base else spread * noise
        out[name] = jnp.asarray(drawn.astype(out[name].dtype))
    for name, factor in factors.items():
        out[name] = (out[name] * factor).astype(out[name].dtype)
    return out
```

```python
from contextlib import ExitStack

import concourse.bass as bass
from concourse import mybir

F32 = mybir.dt.float32
F32R = mybir.dt.float32r
F16 = mybir.dt.float16
I32 = mybir.dt.int32
ALU = mybir.AluOpType
ACT = mybir.ActivationFunctionType
AX = mybir.AxisListType

P = 128
B, L, D = 2, 1024, 256
G, F = 3 * D, 1024
T = 16
C = L // T
R = B * C
KD = D // P
MG = G // P
MF = F // P
assert R == P
N2 = 2 * R
PAIRS = T // 2
COARSE_TAIL = T // 2
COARSE = COARSE_TAIL + T
WARM = COARSE + T
SEAM_TOL = 2.0 ** -19
RELU_ACT = MF // 2
ORDER = [4, 5, 0, 1, 2, 3]
XGROUPS = [4, 5, 6, 7, 0, 1, 2, 3]


def recurrence_ffn_kernel(nc: bass.Bass, x, cond, Wk, Wr, W1, b1, W2, b2, out):
    with ExitStack() as ctx:
        def sb(name, shape, dt=F32):
            return ctx.enter_context(nc.sbuf_tensor(name, shape, dt))

        def psum(name, shape):
            return ctx.enter_context(nc.psum_tensor(name, shape, F32))

        def sem(name):
            return ctx.enter_context(nc.semaphore(name))

        x_rows = sb("x_rows", [P, T, D])
        b2_rows = sb("b2_rows", [P, D])
        x_hi = sb("x_hi", [P, PAIRS * KD * N2], F32R)
        x_lo = sb("x_lo", [P, PAIRS * KD * N2], F32R)
        wk = sb("wk", [P, KD, G])
        wk_hi = sb("wk_hi", [P, KD, G], F32R)
        wk_lo = sb("wk_lo", [P, KD, G], F32R)
        wr = sb("wr", [P, KD, G])
        wr_half = sb("wr_half", [P, KD, G], F16)
        w1 = sb("w1", [P, KD, F])
        w1_hi = sb("w1_hi", [P, KD, F], F32R)
        w1_lo = sb("w1_lo", [P, KD, F], F32R)
        w2 = sb("w2", [P, MF, D])
        w2_hi = sb("w2_hi", [P, MF, D], F32R)
        w2_lo = sb("w2_lo", [P, MF, D], F32R)
        small_rows = sb("small_rows", [MF + B * KD, P])
        small_cols = sb("small_cols", [P, MF + B * KD])
        ident = sb("ident", [P, P])
        ones = sb("ones", [P, 1])
        table_probe = sb("table_probe", [P, 1])

        h_half = sb("h_half", [P, KD, R], F16)
        h_pair = sb("h_pair", [P, KD, 2 * R])
        h_hi = sb("h_hi", [P, KD, 2 * R], F32R)
        h_lo = sb("h_lo", [P, KD, 2 * R], F32R)
        c = sb("c", [P, KD, R])
        h_seam = sb("h_seam", [P, KD, R])
        c_seam = sb("c_seam", [P, KD, R])
        tanh_g = sb("tanh_g", [P, KD, R])
        sig_f = sb("sig_f", [P, KD, R])
        sig_o = sb("sig_o", [P, KD, R])
        tanh_c = sb("tanh_c", [P, KD, R])
        c_less_g = sb("c_less_g", [P, KD, R])
        kept = sb("kept", [P, KD, R])
        relu = sb("relu", [P, MF, N2])
        relu_hi = sb("relu_hi", [P, MF, N2], F32R)
        relu_lo = sb("relu_lo", [P, MF, N2], F32R)
        y = sb("y", [P, T, D])
        gap = sb("gap", [P, 2, KD, B, C - 1])
        gap_sq = sb("gap_sq", [P, 2 * KD * B * (C - 1)])
        row_ok = sb("row_ok", [P, 1])
        redo = sb("redo", [1, 1], I32)

        gates = psum("gates", [P, MG * N2])
        inner = psum("inner", [P, MF * N2])
        ffn_out = psum("ffn_out", [P, 512])
        ok_count = gates

        small_in, wk_in, wr_in, w1_in, w2_in, b2_in = (
            sem(n) for n in ("small_in", "wk_in", "wr_in", "w1_in", "w2_in", "b2_in"))
        table_loaded = sem("table_loaded")
        x_in = [sem(f"x_in{n}") for n in range(2)]
        ident_zero, ident_ready, ones_ready = (sem(n) for n in ("ident_zero", "ident_ready", "ones_ready"))
        small_turned, small_copied = sem("small_turned"), sem("small_copied")
        x_turned, x_hi_ready, x_lo_ready = (sem(n) for n in ("x_turned", "x_hi_ready", "x_lo_ready"))
        wk_hi_ready, wk_lo_ready, wr_half_ready = (sem(n) for n in ("wk_hi_ready", "wk_lo_ready", "wr_half_ready"))
        w1_hi_ready, w1_lo_ready, w2_hi_ready, w2_lo_ready = (
            sem(n) for n in ("w1_hi_ready", "w1_lo_ready", "w2_hi_ready", "w2_lo_ready"))
        xb_ready, zero_state = sem("xb_ready"), sem("zero_state")
        g_ready, f_ready, o_ready = sem("g_ready"), sem("f_ready"), sem("o_ready")
        tanh_g_done, sig_f_done, sig_o_done, tanh_c_done = (
            sem(n) for n in ("tanh_g_done", "sig_f_done", "sig_o_done", "tanh_c_done"))
        less_done, kept_done, c_done, h_done = (sem(n) for n in ("less_done", "kept_done", "c_done", "h_done"))
        seam_done = sem("seam_done")
        h_hi_done, h_split = sem("h_hi_done"), sem("h_split")
        inner_ready = sem("inner_ready")
        relu_act, relu_dve = sem("relu_act"), sem("relu_dve")
        relu_hi_done, relu_split = sem("relu_hi_done"), sem("relu_split")
        out_ready, y_ready = sem("out_ready"), sem("y_ready")
        stored = sem("stored")
        check_step, ok_counted, redo_ready = sem("check_step"), sem("ok_counted"), sem("redo_ready")

        x_view = x.rearrange("b (c t) d -> (b c) t d", t=T)
        out_view = out.rearrange("b (c t) d -> (b c) t d", t=T)
        banks = [gates, inner]

        def halves(p):
            return slice(p * R, (p + 1) * R)

        def gate_step(bank, first, p):
            return bank[:, first * N2:(first + KD) * N2].rearrange("q (m t) -> q m t", t=N2)[:, :, halves(p)]

        def split_seq(ap):
            return ap.rearrange("q k (b c) -> q k b c", b=B)

        block = ctx.enter_context(nc.Block())

        @block.sync
        def _(sp):
            sp.dma_start(small_rows[0:MF, :], b1.rearrange("(m p) -> m p", p=P)).then_inc(small_in, 16)
            sp.dma_start(small_rows[MF:, :], cond.rearrange("b (k p) -> (b k) p", p=P)).then_inc(small_in, 16)
            for n, (lo, hi) in enumerate([(T // 2, T), (0, T // 2)]):
                sp.dma_start(x_rows[:, lo:hi, :], x_view[:, lo:hi, :]).then_inc(x_in[n], 16)
            sp.dma_start(w1[:, :, :], W1.rearrange("(k p) n -> p k n", p=P)).then_inc(w1_in, 16)
            sp.dma_start(w2[:, :, :], W2.rearrange("(k p) n -> p k n", p=P)).then_inc(w2_in, 16)

            def sweep(k):
                with sp.Fori(0, PAIRS) as i:
                    sp.wait_ge(y_ready, k * PAIRS + i + 1)
                    sp.dma_start(out_view[:, bass.ds(i * 2, 2), :], y[:, bass.ds(i * 2, 2), :]).then_inc(stored, 16)

            sweep(0)
            sp.wait_ge(redo_ready, 1)
            with sp.If(sp.value_load(redo[0:1, 0:1], min_val=0, max_val=1) != 0):
                with sp.Fori(1, C) as k:
                    sweep(k)
                sp.wait_ge(stored, 16 * PAIRS * C)
            sp.wait_ge(stored, 16 * PAIRS)

        @block.gpsimd
        def _(pool):
            pool.dma_start(b2_rows[:, :], b2.partition_broadcast(P)).then_inc(b2_in, 16)
            nc.gpsimd.memset(ident[:, :], 0.0).then_inc(ident_zero, 1)
            pool.wait_ge(ident_zero, 1)
            nc.gpsimd.affine_select(out=ident[:, :], in_=ident[:, :], compare_op=ALU.not_equal, fill=1.0,
                                    base=0, pattern=[[-1, P]], channel_multiplier=1).then_inc(ident_ready, 1)
            nc.gpsimd.memset(ones[:, :], 1.0).then_inc(ones_ready, 1)
            pool.wait_ge(b2_in, 16)
            for n, g in enumerate(XGROUPS):
                pool.wait_ge(x_turned, n + 1)
                for s in range(2):
                    rows = x_rows[:, 2 * g + s, :]
                    nc.gpsimd.tensor_tensor(rows, rows, b2_rows[:, :], ALU.add).then_inc(xb_ready, 1)

        @block.scalar
        def _(act):
            act.dma_start(wk[:, :, :], Wk.rearrange("(k p) n -> p k n", p=P)).then_inc(wk_in, 16)
            act.dma_start(wr[:, :, :], Wr.rearrange("(k p) n -> p k n", p=P)).then_inc(wr_in, 16)
            act.wait_ge(ones_ready, 1)
            nc.scalar.activation(table_probe[:, :], ones[:, :], ACT.Sigmoid).then_inc(table_loaded, 1)
            act.wait_ge(wk_in, 16)
            nc.scalar.copy(wk_hi[:, :, :], wk[:, :, :]).then_inc(wk_hi_ready, 1)
            act.wait_ge(wr_in, 16)
            nc.scalar.copy(wr_half[:, :, :], wr[:, :, :]).then_inc(wr_half_ready, 1)
            for n, g in enumerate(XGROUPS):
                act.wait_ge(x_turned, n + 1)
                nc.scalar.copy(x_hi[:, g * 512:(g + 1) * 512],
                               inner[:, n % 2 * 512:(n % 2 + 1) * 512]).then_inc(x_hi_ready, 1)
            act.wait_ge(w1_in, 16)
            nc.scalar.copy(w1_hi[:, :, :], w1[:, :, :]).then_inc(w1_hi_ready, 1)
            act.wait_ge(w2_in, 16)
            nc.scalar.copy(w2_hi[:, :, :], w2[:, :, :]).then_inc(w2_hi_ready, 1)

            def step(count, bank, p):
                act.wait_ge(g_ready, count)
                nc.scalar.activation(tanh_g[:, :, :], gate_step(bank, 0, p), ACT.Tanh).then_inc(tanh_g_done, 1)
                act.wait_ge(f_ready, count)
                nc.scalar.activation(sig_f[:, :, :], gate_step(bank, KD, p), ACT.Sigmoid).then_inc(sig_f_done, 1)
                act.wait_ge(o_ready, count)
                nc.scalar.activation(sig_o[:, :, :], gate_step(bank, 2 * KD, p), ACT.Sigmoid).then_inc(sig_o_done, 1)
                act.wait_ge(c_done, count)
                nc.scalar.activation(tanh_c[:, :, :], c[:, :, :], ACT.Tanh).then_inc(tanh_c_done, 1)

            def relus(first_pair_count):
                act.wait_ge(inner_ready, first_pair_count + RELU_ACT)
                for m in range(RELU_ACT):
                    last = nc.scalar.activation(relu[:, m, :], inner[:, m * N2:(m + 1) * N2], ACT.Relu,
                                                bias=small_cols[:, m:m + 1])
                last.then_inc(relu_act, 1)

            def quad(count):
                for s in range(4):
                    step(count + s + 1, banks[s // 2], s % 2)

            with act.Fori(0, WARM // 4) as i:
                quad(i * 4)

            act.wait_ge(small_copied, 1)
            def sweep(k):
                base = WARM + k * T
                for p in range(2):
                    step(base + p + 1, gates, p)
                with act.Fori(1, PAIRS) as i:
                    for p in range(2):
                        step(base + i * 2 + p + 1, gates, p)
                    relus((k * PAIRS + i - 1) * MF)
                relus((k * PAIRS + PAIRS - 1) * MF)

            sweep(0)
            act.wait_ge(redo_ready, 1)
            with act.If(act.value_load(redo[0:1, 0:1], min_val=0, max_val=1) != 0):
                with act.Fori(1, C) as k:
                    sweep(k)

        @block.vector
        def _(dve):
            nc.vector.memset(h_half[:, :, :], 0.0).then_inc(zero_state, 1)
            nc.vector.memset(c[:, :, :], 0.0).then_inc(zero_state, 1)
            dve.wait_ge(small_turned, 1)
            nc.vector.tensor_copy(small_cols[:, :], ffn_out[:, 0:MF + B * KD]).then_inc(small_copied, 1)
            dve.wait_ge(wk_in, 16)
            dve.wait_ge(wk_hi_ready, 1)
            nc.vector.tensor_tensor(wk_lo[:, :, :], wk[:, :, :], wk_hi[:, :, :].bitcast(F32),
                                    ALU.subtract).then_inc(wk_lo_ready, 1)
            for n, g in enumerate(XGROUPS):
                dve.wait_ge(x_hi_ready, n + 1)
                nc.vector.tensor_tensor(x_lo[:, g * 512:(g + 1) * 512],
                                        inner[:, n % 2 * 512:(n % 2 + 1) * 512],
                                        x_hi[:, g * 512:(g + 1) * 512].bitcast(F32),
                                        ALU.subtract).then_inc(x_lo_ready, 1)
            dve.wait_ge(w1_hi_ready, 1)
            nc.vector.tensor_tensor(w1_lo[:, :, :], w1[:, :, :], w1_hi[:, :, :].bitcast(F32),
                                    ALU.subtract).then_inc(w1_lo_ready, 1)
            dve.wait_ge(w2_hi_ready, 1)
            nc.vector.tensor_tensor(w2_lo[:, :, :], w2[:, :, :], w2_hi[:, :, :].bitcast(F32),
                                    ALU.subtract).then_inc(w2_lo_ready, 1)
            dve.wait_ge(zero_state, 2)

            cond_cols = small_cols[:, MF:].rearrange("q (b k) -> q k b", b=B)

            def step(count, h_out, shift=False):
                src, dst = (slice(0, C - 1), slice(1, C)) if shift else (slice(0, C), slice(0, C))
                dve.wait_ge(tanh_g_done, count)
                nc.vector.tensor_tensor(c_less_g[:, :, :], c[:, :, :], tanh_g[:, :, :],
                                        ALU.subtract).then_inc(less_done, 1)
                dve.wait_ge(less_done, count)
                dve.wait_ge(sig_f_done, count)
                nc.vector.tensor_tensor(kept[:, :, :], c_less_g[:, :, :], sig_f[:, :, :],
                                        ALU.mult).then_inc(kept_done, 1)
                dve.wait_ge(kept_done, count)
                nc.vector.tensor_tensor(c[:, :, :], kept[:, :, :], tanh_g[:, :, :], ALU.add).then_inc(c_done, 1)
                dve.wait_ge(sig_o_done, count)
                dve.wait_ge(tanh_c_done, count)
                if not shift:
                    nc.vector.tensor_tensor(h_out, sig_o[:, :, :], tanh_c[:, :, :], ALU.mult).then_inc(h_done, 1)
                    return
                nc.vector.tensor_tensor(split_seq(h_out)[:, :, :, dst], split_seq(sig_o[:, :, :])[:, :, :, src],
                                        split_seq(tanh_c[:, :, :])[:, :, :, src], ALU.mult)
                nc.vector.tensor_copy(split_seq(h_out)[:, :, :, 0], cond_cols)
                dve.wait_ge(kept_done, count)
                nc.vector.tensor_tensor(split_seq(c[:, :, :])[:, :, :, dst], split_seq(kept[:, :, :])[:, :, :, src],
                                        split_seq(tanh_g[:, :, :])[:, :, :, src], ALU.add)
                nc.vector.tensor_copy(split_seq(c[:, :, :])[:, :, :, 0], cond_cols).then_inc(h_done, 1)
                dve.wait_ge(h_done, count)

            def keep_seam(count):
                nc.vector.tensor_copy(h_seam[:, :, :], h_pair[:, :, halves(1)]).then_inc(seam_done, 1)
                nc.vector.tensor_copy(c_seam[:, :, :], c[:, :, :]).then_inc(seam_done, 1)
                dve.wait_ge(seam_done, count)

            def quads(first, last, h_of):
                with dve.Fori(first // 4, last // 4 - 1) as i:
                    for s in range(4):
                        step(i * 4 + s + 1, h_of(s % 2))
                for s in range(last - 4, last - 1):
                    step(s + 1, h_of(s % 2))

            def coarse_h(p):
                return h_half[:, :, :]

            def fine_h(p):
                return h_pair[:, :, halves(p)]

            dve.wait_ge(small_copied, 1)
            quads(0, COARSE_TAIL, coarse_h)
            step(COARSE_TAIL, h_half[:, :, :], shift=True)
            quads(COARSE_TAIL, COARSE, coarse_h)
            step(COARSE, fine_h(1), shift=True)
            quads(COARSE, WARM, fine_h)
            step(WARM, fine_h(1), shift=True)
            keep_seam(2)

            def split_h(count):
                nc.vector.tensor_copy(h_hi[:, :, :], h_pair[:, :, :]).then_inc(h_hi_done, 1)
                dve.wait_ge(h_hi_done, count)
                nc.vector.tensor_tensor(h_lo[:, :, :], h_pair[:, :, :], h_hi[:, :, :].bitcast(F32),
                                        ALU.subtract).then_inc(h_split, 1)

            def relus(pairs):
                dve.wait_ge(inner_ready, pairs * MF + MF)
                for m in range(RELU_ACT, MF):
                    last = nc.vector.tensor_scalar(relu[:, m, :], inner[:, m * N2:(m + 1) * N2],
                                                   small_cols[:, m:m + 1], 0.0, ALU.add, ALU.max)
                last.then_inc(relu_dve, 1)

            def split_relu(count):
                dve.wait_ge(relu_act, count)
                dve.wait_ge(relu_dve, count)
                nc.vector.tensor_copy(relu_hi[:, :, :], relu[:, :, :]).then_inc(relu_hi_done, 1)
                dve.wait_ge(relu_hi_done, count)
                nc.vector.tensor_tensor(relu_lo[:, :, :], relu[:, :, :], relu_hi[:, :, :].bitcast(F32),
                                        ALU.subtract).then_inc(relu_split, 1)

            def residual(pair, count):
                dve.wait_ge(out_ready, count)
                nc.vector.tensor_tensor(y[:, bass.ds(pair * 2, 2), :], ffn_out[:, :].rearrange("q (a d) -> q a d", a=2),
                                        x_rows[:, bass.ds(pair * 2, 2), :], ALU.add).then_inc(y_ready, 1)

            dve.wait_ge(xb_ready, T)

            def sweep(k, again=False):
                base = WARM + k * T
                done = k * PAIRS
                if again:
                    dve.wait_ge(stored, k * (16 * PAIRS))

                def pair(q, pairs, finish):
                    step(q + 1, fine_h(0))
                    if finish is not None:
                        residual(finish, pairs - 1)
                    step(q + 2, fine_h(1))
                    dve.wait_ge(h_done, q + 2)
                    if pairs is not done:
                        relus(pairs - 1)
                    elif again:
                        dve.wait_ge(inner_ready, pairs * MF)
                    split_h(pairs + 1)
                    if pairs is not done:
                        split_relu(pairs)

                pair(base, done, None)
                pair(base + 2, done + 1, None)
                with dve.Fori(2, PAIRS) as i:
                    pair(i * 2 + base, i + done, i - 2)
                residual(PAIRS - 2, done + PAIRS - 1)
                relus(done + PAIRS - 1)
                split_relu(done + PAIRS)
                residual(PAIRS - 1, done + PAIRS)

            def seams():
                for j, (end, start) in enumerate(((h_pair[:, :, halves(1)], h_seam[:, :, :]),
                                                  (c[:, :, :], c_seam[:, :, :]))):
                    last = nc.vector.tensor_tensor(gap[:, j], split_seq(end)[:, :, :, 0:C - 1],
                                                   split_seq(start)[:, :, :, 1:C], ALU.subtract)
                last.then_inc(check_step, 1)
                dve.wait_ge(check_step, 1)
                flat = gap_ok = gap[:, :, :, :, :].rearrange("q a k b c -> q (a k b c)")
                nc.vector.tensor_tensor(gap_sq[:, :], flat, flat, ALU.mult).then_inc(check_step, 1)
                dve.wait_ge(check_step, 2)
                nc.vector.tensor_scalar(gap_ok, gap_sq[:, :], SEAM_TOL ** 2, None, ALU.is_le).then_inc(check_step, 1)
                dve.wait_ge(check_step, 3)
                nc.vector.tensor_reduce(row_ok[:, :], gap_ok, AX.X, ALU.min).then_inc(check_step, 1)
                dve.wait_ge(ok_counted, 1)
                nc.vector.tensor_scalar(redo[0:1, 0:1], ok_count[0:1, 0:1], float(P), None,
                                        ALU.is_lt).then_inc(redo_ready, 1)

            def reseed(k):
                for end, start in ((h_pair[:, :, halves(1)], h_seam[:, :, :]), (c[:, :, :], c_seam[:, :, :])):
                    last = nc.vector.tensor_copy(split_seq(start)[:, :, :, 1:C], split_seq(end)[:, :, :, 0:C - 1])
                last.then_inc(seam_done, 1)
                dve.wait_ge(seam_done, 2 * k + 1)
                nc.vector.tensor_copy(h_pair[:, :, halves(1)], h_seam[:, :, :])
                nc.vector.tensor_copy(c[:, :, :], c_seam[:, :, :]).then_inc(seam_done, 1)
                dve.wait_ge(seam_done, 2 * k + 2)

            sweep(0)
            seams()
            dve.wait_ge(redo_ready, 1)
            with dve.If(dve.value_load(redo[0:1, 0:1], min_val=0, max_val=1) != 0):
                with dve.Fori(1, C) as k:
                    reseed(k)
                    sweep(k, again=True)

        @block.tensor
        def _(pe):
            pe.wait_ge(ident_ready, 1)
            pe.wait_ge(small_in, 32)
            nc.tensor.transpose(ffn_out[:, 0:MF + B * KD], small_rows[:, :],
                                ident[0:MF + B * KD, 0:MF + B * KD]).then_inc(small_turned, 1)
            for n, g in enumerate(XGROUPS):
                pe.wait_ge(x_in[0 if g >= PAIRS // 2 else 1], 16)
                if n >= 2:
                    pe.wait_ge(x_lo_ready, n - 1)
                for j in range(4):
                    at = n % 2 * 512 + j * P
                    last = nc.tensor.transpose(inner[:, at:at + P], x_rows[:, 2 * g + j % 2, j // 2 * P:(j // 2 + 1) * P],
                                               ident[:, :])
                last.then_inc(x_turned, 1)

            def x_gates(pair, bank, parts, blocks=ORDER):
                for m in blocks:
                    at = (m + 2) % MG * N2
                    for k in range(KD):
                        for j, (w, v) in enumerate(parts):
                            nc.tensor.matmul(bank[:, at:at + N2], w[:, k, m * P:(m + 1) * P],
                                             v[:, bass.ds((pair * KD + k) * N2, N2)],
                                             start=(m % KD == 0 and k == 0 and j == 0), stop=False,
                                             skip_group_check=True)

            def h_gates(bank, p, w, h):
                for m in ORDER:
                    at = (m + 2) % MG * N2 + p * R
                    for k in range(KD):
                        last = nc.tensor.matmul(bank[:, at:at + R], w[:, k, m * P:(m + 1) * P],
                                                h[:, k, :], start=False, stop=True, skip_group_check=True)
                    if m % KD == KD - 1:
                        last.then_inc((f_ready, o_ready, g_ready)[m // KD], 1)

            HIGH = [(wk_hi, x_hi)]
            FULL = [(wk_hi, x_hi), (wk_hi, x_lo), (wk_lo, x_hi)]

            def fine_h(p):
                return h_pair[:, :, halves(1 - p)]

            def coarse_h(p):
                return h_half

            def warm_pair(following, count, pp, w, h_of, parts, first=False):
                for p, blocks in enumerate((ORDER[:MG // 2], ORDER[MG // 2:])):
                    if not (first and p == 0):
                        pe.wait_ge(h_done, count + p)
                    h_gates(banks[pp], p, w, h_of(p))
                    x_gates(following, banks[1 - pp], parts, blocks)

            pe.wait_ge(wk_hi_ready, 1)
            pe.wait_ge(wr_half_ready, 1)
            pe.wait_ge(zero_state, 2)
            pe.wait_ge(x_hi_ready, len(XGROUPS))
            pe.wait_ge(x_lo_ready, len(XGROUPS))
            x_gates(PAIRS - COARSE_TAIL // 2, banks[0], HIGH)
            for n in range(COARSE_TAIL // 2):
                warm_pair((PAIRS - COARSE_TAIL // 2 + n + 1) % PAIRS, 2 * n, n % 2, wr_half, coarse_h, HIGH,
                          first=(n == 0))
            with pe.Fori(0, T // 4 - 1) as i:
                for pp in range(2):
                    warm_pair(i * 2 + pp + 1, i * 4 + COARSE_TAIL + 2 * pp, pp, wr_half, coarse_h, HIGH)
            warm_pair(PAIRS - 1, COARSE - 4, 0, wr_half, coarse_h, HIGH)
            pe.wait_ge(wk_lo_ready, 1)
            warm_pair(0, COARSE - 2, 1, wr_half, coarse_h, FULL)
            with pe.Fori(0, T // 4 - 1) as i:
                for pp in range(2):
                    warm_pair(i * 2 + pp + 1, i * 4 + COARSE + 2 * pp, pp, wr, fine_h, FULL)
            warm_pair(PAIRS - 1, WARM - 4, 0, wr, fine_h, FULL)
            warm_pair(0, WARM - 2, 1, wr, fine_h, FULL)

            pe.wait_ge(w1_lo_ready, 1)
            pe.wait_ge(w2_lo_ready, 1)

            def inner_product(count):
                pe.wait_ge(h_split, count)
                for m in range(MF):
                    n = 0
                    for k in range(KD):
                        for w, v in ((w1_hi, h_hi), (w1_hi, h_lo), (w1_lo, h_hi)):
                            last = nc.tensor.matmul(inner[:, m * N2:(m + 1) * N2], w[:, k, m * P:(m + 1) * P],
                                                    v[:, k, :], start=(n == 0), stop=(n == 3 * KD - 1))
                            n += 1
                    last.then_inc(inner_ready, 1)

            def outer_product(count, wait_y=True):
                pe.wait_ge(relu_split, count)
                if wait_y:
                    pe.wait_ge(y_ready, count - 1)
                for t in range(2):
                    for m in range(MF):
                        for j, (v, w) in enumerate(((relu_hi, w2_hi), (relu_hi, w2_lo), (relu_lo, w2_hi))):
                            last = nc.tensor.matmul(ffn_out[:, t * D:(t + 1) * D], v[:, m, t * R:(t + 1) * R], w[:, m, :],
                                                    start=(m == 0 and j == 0), stop=(m == MF - 1 and j == 2))
                last.then_inc(out_ready, 1)

            def sweep_pair(pair, steps, pairs, outer, inner_, wait_y=True):
                if pair is not None:
                    pe.wait_ge(sig_o_done, steps)
                    x_gates(pair, gates, FULL)
                pe.wait_ge(h_done, steps)
                h_gates(gates, 0, wr, fine_h(0))
                if outer:
                    outer_product(pairs - 1, wait_y)
                pe.wait_ge(h_done, steps + 1)
                h_gates(gates, 1, wr, fine_h(1))
                if inner_:
                    inner_product(pairs)

            def sweep(k, again=False):
                base, done = WARM + k * T, k * PAIRS
                if again:
                    pe.wait_ge(seam_done, k * 2 + 2)
                    x_gates(0, gates, FULL)
                sweep_pair(None, base, done, False, False)
                sweep_pair(1, base + 2, done + 1, False, True)
                sweep_pair(2, base + 4, done + 2, True, True, wait_y=again)
                with pe.Fori(3, PAIRS) as i:
                    sweep_pair(i, i * 2 + base, i + done, True, True)
                outer_product(done + PAIRS - 1)
                inner_product(done + PAIRS)
                outer_product(done + PAIRS)

            sweep(0)
            pe.wait_ge(ones_ready, 1)
            pe.wait_ge(check_step, 4)
            nc.tensor.matmul(ok_count[0:1, 0:1], row_ok[:, :], ones[:, :], start=True, stop=True).then_inc(ok_counted, 1)
            pe.wait_ge(redo_ready, 1)
            with pe.If(pe.value_load(redo[0:1, 0:1], min_val=0, max_val=1) != 0):
                with pe.Fori(1, C) as k:
                    sweep(k, again=True)


_INS = ['x', 'cond_1024', 'L0_cond_Wk', 'L0_cond_Wr', 'L0_ffn_W1', 'L0_ffn_b1', 'L0_ffn_W2', 'L0_ffn_b2']
_OUTS = [((B, L, D), 'float32')]


def kernel(**inputs):
    import numpy as _np
    import concourse.bacc as _bacc
    from concourse import mybir as _mybir
    from concourse.bass_utils import run_bass_kernel_spmd as _run

    nc = _bacc.Bacc("TRN2", target_bir_lowering=False, num_devices=1)
    arrays, args = {}, []
    for name in _INS:
        a = _np.ascontiguousarray(inputs[name])
        arrays[f"in_{name}_dram"] = a
        args.append(nc.dram_tensor(f"in_{name}_dram", a.shape, _mybir.dt.from_np(a.dtype), kind="ExternalInput").ap())
    for i, (shape, dtype) in enumerate(_OUTS):
        dt = _mybir.dt.from_np(_np.dtype(dtype))
        args.append(nc.dram_tensor(f"out_{i}_dram", shape, dt, kind="ExternalOutput").ap())
    recurrence_ffn_kernel(nc, *args)
    r = _run(nc, [arrays], core_ids=[0])
    return r.results[0]["out_0_dram"]
```
